# Optimizing a Trainium2 kernel written in Bass

```python
import numpy as np
import jax
import jax.numpy as jnp

def _softmax(x, axis=-1):
    return jax.nn.softmax(x, axis=axis)

def _gelu(x):
    return jax.nn.gelu(x, approximate=True)

def _silu(x):
    return jax.nn.silu(x)

def _sigmoid(x):
    return jax.nn.sigmoid(x)

def _layernorm(x, axis=-1, eps=1e-05):
    m = jnp.mean(x, axis=axis, keepdims=True)
    v = jnp.var(x, axis=axis, keepdims=True)
    return (x - m) / jnp.sqrt(v + eps)

def _scatter_add(tgt, idx, src, axis=0):
    return tgt.at[idx].add(src)

def _segment_sum(src, seg, n):
    return jax.ops.segment_sum(src, seg, n)
kernel_name = 'mk_adj_preln_d4_adj_r2_7409bd'

def setup_inputs(seed: int=0):
    np.random.seed(seed)
    _w = jnp.asarray

    def _rec_inputs():
        import jax
        import jax.numpy as jnp
        _gk = jax.random.key(seed)
        x = -0.0002928 + 1 * jax.random.normal(jax.random.fold_in(_gk, 1), (4096, 256), jnp.float32)
        _w = (1.0 + jnp.arange(4096, dtype=jnp.float32)) ** (-0.5)
        _w = _w / _w.mean()
        _pij = jnp.clip(0.00195312 * _w[:, None] * _w[None, :], 0.0, 1.0)
        _a = jax.random.uniform(jax.random.fold_in(_gk, 2), (4096, 4096)) < _pij
        _a = jnp.logical_or(_a, jnp.eye(4096, dtype=bool))
        _af = _a.astype(jnp.float32)
        adj = _af
        return (x, adj)
    x, adj = _rec_inputs()

    def _L0_gnn_setup():
        import jax, jax.numpy as jnp
        import numpy as np
        N = 4096
        F_IN = 256
        F_OUT = 256
        DENSITY = 0.01
        key = jax.random.key(seed)
        k_x, k_adj, k_w, k_b = jax.random.split(key, 4)
        input_features = jax.random.normal(k_x, (N, F_IN), dtype=jnp.float32)
        adj = (jax.random.uniform(k_adj, (N, N)) < DENSITY).astype(jnp.float32)
        idx = jnp.arange(N)
        adj = adj.at[idx, idx].set(1.0)
        W = jax.random.normal(k_w, (F_IN, F_OUT), dtype=jnp.float32) / np.sqrt(F_IN)
        b = jax.random.normal(k_b, (F_OUT,), dtype=jnp.float32) * 0.01
        return {'input_features': input_features, 'adj': adj, 'W': W, 'b': b}
    _L0_gnn_all = _L0_gnn_setup()
    _L0_gnn_in = {k: v for k, v in _L0_gnn_all.items() if k in ('W', 'b')}
    del _L0_gnn_all

    def _L1_gnn_setup():
        import jax, jax.numpy as jnp
        import numpy as np
        N = 4096
        IN_F = 256
        OUT_F = 256
        key = jax.random.key(seed)
        k_x, k_adj, k_w = jax.random.split(key, 3)
        x = jax.random.normal(k_x, (N, IN_F), dtype=jnp.float32)
        adj = jax.random.uniform(k_adj, (N, N), dtype=jnp.float32)
        stdv = 1.0 / np.sqrt(OUT_F)
        weight = jax.random.uniform(k_w, (IN_F, OUT_F), dtype=jnp.float32, minval=-stdv, maxval=stdv)
        return {'x': x, 'adj': adj, 'weight': weight}
    _L1_gnn_all = _L1_gnn_setup()
    _L1_gnn_in = {k: v for k, v in _L1_gnn_all.items() if k in ('weight',)}
    del _L1_gnn_all

    def _L2_gnn_setup():
        import jax, jax.numpy as jnp
        import numpy as np
        N = 4096
        DIN = 256
        DOUT = 256
        TAU = 1.0
        EPS = 1e-08
        NORM_EPS = 1e-08
        key = jax.random.key(seed)
        k1, k2, k3 = jax.random.split(key, 3)
        x = jax.random.normal(k1, (N, DIN), dtype=jnp.float32)
        adj = jax.random.uniform(k2, (N, N), dtype=jnp.float32)
        limit = float(np.sqrt(6.0 / (DIN + DOUT)))
        weight = jax.random.uniform(k3, (DIN, DOUT), dtype=jnp.float32, minval=-limit, maxval=limit)
        bias = jnp.zeros((DOUT,), dtype=jnp.float32)
        return {'x': x, 'adj': adj, 'weight': weight, 'bias': bias}
    _L2_gnn_all = _L2_gnn_setup()
    _L2_gnn_in = {k: v for k, v in _L2_gnn_all.items() if k in ('weight', 'bias')}
    del _L2_gnn_all

    def _L3_gnn_setup():
        import jax, jax.numpy as jnp
        import numpy as np
        N = 4096
        D = 256
        EPS = 1e-12
        key = jax.random.key(seed)
        k1, k2 = jax.random.split(key)
        cur = jax.random.normal(k1, (N, D), dtype=jnp.float32)
        incidence_m = jax.random.normal(k2, (N, N), dtype=jnp.float32)
        return {'cur': cur, 'incidence_m': incidence_m}
    _L3_gnn_all = _L3_gnn_setup()
    _L3_gnn_in = {k: v for k, v in _L3_gnn_all.items() if k in ()}
    del _L3_gnn_all
    return {'x': x, 'adj': adj, 'L0_gnn_W': _L0_gnn_in['W'], 'L0_gnn_b': _L0_gnn_in['b'], 'L1_gnn_weight': _L1_gnn_in['weight'], 'L2_gnn_weight': _L2_gnn_in['weight'], 'L2_gnn_bias': _L2_gnn_in['bias']}

def reference(x, adj, L0_gnn_W, L0_gnn_b, L1_gnn_weight, L2_gnn_weight, L2_gnn_bias):
    import jax
    import jax.numpy as jnp

    def _L0_gnn_ref(input_features, adj, W, b):
        import jax, jax.numpy as jnp
        import numpy as np
        N = 4096
        F_IN = 256
        F_OUT = 256
        DENSITY = 0.01
        A = (adj != 0).astype(input_features.dtype)
        hidden = input_features @ W + b
        deg = jnp.sum(A, axis=0)
        return A @ hidden / deg[:, None]

    def _L1_gnn_ref(x, adj, weight):
        import jax, jax.numpy as jnp
        import numpy as np
        N = 4096
        IN_F = 256
        OUT_F = 256
        n = adj.shape[0]
        adj_hat = adj + jnp.eye(n, dtype=adj.dtype)
        rowsum = adj_hat.sum(axis=1)
        d_inv_sqrt = jnp.power(rowsum, -0.5)
        d_inv_sqrt = jnp.where(jnp.isinf(d_inv_sqrt), 0.0, d_inv_sqrt)
        adj_norm = adj_hat * d_inv_sqrt[:, None] * d_inv_sqrt[None, :]
        support = x @ weight
        out = adj_norm @ support
        return jax.nn.relu(out)

    def _L2_gnn_ref(x, adj, weight, bias):
        import jax, jax.numpy as jnp
        import numpy as np
        N = 4096
        DIN = 256
        DOUT = 256
        TAU = 1.0
        EPS = 1e-08
        NORM_EPS = 1e-08
        h = x @ weight
        norm = jnp.linalg.norm(h, axis=1, keepdims=True)
        h_norm = h / jnp.maximum(norm, NORM_EPS)
        sim = h_norm @ h_norm.T
        attn_logits = sim / TAU + jnp.log(adj + EPS)
        attn = jax.nn.softmax(attn_logits, axis=1)
        out = attn @ h + bias
        return out

    def _L3_gnn_ref(cur, incidence_m):
        import jax, jax.numpy as jnp
        import numpy as np
        N = 4096
        D = 256
        EPS = 1e-12
        mask = incidence_m > 0
        head = jax.lax.stop_gradient(mask.astype(incidence_m.dtype))
        head = head / jnp.maximum(jnp.sqrt(jnp.sum(head * head, axis=-1, keepdims=True)), EPS)
        inc = incidence_m + head
        edge_fea = inc @ cur
        edge_degree = jnp.sum(inc, axis=-1, keepdims=True)
        return edge_fea / edge_degree
    h = jnp.maximum(_layernorm(x, axis=-1), 0.0)
    x = x + _L0_gnn_ref(h, adj, L0_gnn_W, L0_gnn_b)
    h = jnp.maximum(_layernorm(x, axis=-1), 0.0)
    x = x + _L1_gnn_ref(h, adj, L1_gnn_weight)
    h = jnp.maximum(_layernorm(x, axis=-1), 0.0)
    x = x + _L2_gnn_ref(h, adj, L2_gnn_weight, L2_gnn_bias)
    h = jnp.maximum(_layernorm(x, axis=-1), 0.0)
    x = x + _L3_gnn_ref(h, adj)
    return x

_drawn_inputs = setup_inputs


def setup_inputs(seed=0):
    import zlib

    import numpy as np

    out = dict(_drawn_inputs(seed))
    spreads = {'L2_gnn_bias': (0.0, 0.1)}
    factors = {'L0_gnn_b': 5.966}
    for name, (base, spread) in spreads.items():
        noise = np.random.default_rng([zlib.crc32(name.encode()), seed]).standard_normal(out[name].shape)
        drawn = base * np.exp(spread * noise) if base else spread * noise
        out[name] = jnp.asarray(drawn.astype(out[name].dtype))
    for name, factor in factors.items():
        out[name] = (out[name] * factor).astype(out[name].dtype)
    return out
```

```python
import concourse.bass as bass
from concourse import mybir
from contextlib import ExitStack

P = 128
F32 = mybir.dt.float32
F16 = mybir.dt.float16
I32 = mybir.dt.int32
ALU = mybir.AluOpType
ACT = mybir.ActivationFunctionType
AX = mybir.AxisListType
RMAX = bass.bass_isa.ReduceOp.max

LN_EPS = 1e-5
ATTN_EPS = 1e-8
NORM_EPS = 1e-8
HEAD_EPS = 1e-12
ASC = 2.0 ** 14
VSC = 16.0
EXPONENT_BITS = 0x7F800000

SEMS = """w_loaded b_loaded bias_loaded wmax_part wmax_all p2_clamped p2_masked p2_inv thr_step scaled_w
ident_zero ident_f ident_16 one_16 cast_done ones_set half_set deg_zero part_sum at_ready0 acc_done0
y_saved deg_added cnt_ready f0_ready cnt1_ready dinv_ready s1_ready r3_clamped r3_ready f3_a f3_b
f3_c f3_ready relu1 epi_done1 acc_done1 x_biased sumsq_ready ss_clamped inv_ready hn_ready tn_done
hnhi_ready hnt_ready s_done exp_done p_done phi_done p_ready pv_done rden_ready rsc_ready epi_done2
acc_done3 epi_done3 out_stored x1_ready""".split()
PREP_SEMS = "bn_done aggr_done var_ready rstd_ready xn_ready tp_done ht_ready o_done s_ready hi_ready val_ready".split()


def since(eng, sem, count):
    if isinstance(count, int) and count <= 0:
        return
    eng.wait_ge(sem, count)


def steps(eng, n, unroll, lag, body):
    head = -(-(lag + 2) // unroll) * unroll
    for k in range(head):
        body(k, k % unroll, lambda d, k=k: 0 <= k - d < n)
    if n > head:
        with eng.Fori(head, n - unroll + 1, unroll) as k0:
            for u in range(unroll):
                body(k0 + u, u, lambda d: True)
    for k in range(max(n, head), n + lag):
        body(k, k % unroll, lambda d, k=k: 0 <= k - d < n)


def gnn_kernel(nc, x, adj, w0, b0, w1, w2, bias2, out):
    N, D = x.shape
    NB = N // P
    C = D // P
    GB = 4
    NG = NB // GB
    TQ = 8
    NQ = NB // TQ
    assert D == 256 and N % 512 == 0

    x_v = x.rearrange("(t p) d -> p t d", p=P)
    adj_v = adj.rearrange("(t p) j -> t p j", p=P)
    out_v = out.rearrange("(t p) d -> t p d", p=P)
    at_dram = nc.dram_tensor("at_dram", (NB, P, N), F16, kind="Internal").ap()

    with ExitStack() as ctx:
        def sb(name, shape, dt):
            return ctx.enter_context(nc.sbuf_tensor(name, shape, dt))

        sem = {n: ctx.enter_context(nc.semaphore(n)) for n in SEMS}
        prep = [{n: ctx.enter_context(nc.semaphore(f"{n}_{l}")) for n in PREP_SEMS} for l in range(4)]
        x_loaded = [ctx.enter_context(nc.semaphore(f"x_loaded{i}")) for i in range(4)]
        adj_loaded = [ctx.enter_context(nc.semaphore(f"adj_loaded{i}")) for i in range(2)]
        tq_done = ctx.enter_context(nc.semaphore("tq_done"))
        at_stored = [ctx.enter_context(nc.semaphore(f"at_stored{i}")) for i in range(2)]
        a1_loaded = [ctx.enter_context(nc.semaphore(f"a1_loaded{i}")) for i in range(4)]
        a2_loaded = [ctx.enter_context(nc.semaphore(f"a2_loaded{i}")) for i in range(2)]
        a3_loaded = [ctx.enter_context(nc.semaphore(f"a3_loaded{i}")) for i in range(4)]

        xs = sb("xs", [P, NB, D], F32)
        HW = D + 2
        val_hi = [sb(f"val_hi{i}", [P, NB, HW], F16) for i in range(2)]
        val_lo = [sb(f"val_lo{i}", [P, NB, D], F16) for i in range(2)]
        hnt = sb("hnt", [P, 2, C, N], F16)
        y0 = hnt[:, :, :, :].rearrange("p a c n -> p (a c n)").bitcast(F32).rearrange("p (t d) -> p t d", d=D)
        ring = sb("ring", [P, 8 * N], F16)
        stage = [ring[:, i * 2 * N:(i + 1) * 2 * N].bitcast(F32) for i in range(2)]
        at16 = [ring[:, (4 + i) * N:(5 + i) * N] for i in range(2)]
        cast16 = [ring[:, (6 + i) * N:(7 + i) * N] for i in range(2)]
        b0_bc = ring[:, 6 * N:6 * N + 2 * D].bitcast(F32)
        slot1 = [ring[:, i * N:(i + 1) * N] for i in range(4)]
        slot3 = [ring[:, (4 + i) * N:(5 + i) * N] for i in range(4)]
        group = [ring[:, 4 * N:8 * N].rearrange("p (b j i) -> p b j i", b=GB, i=P),
                 ring[:, 0:4 * N].rearrange("p (b j i) -> p b j i", b=GB, i=P)]
        w_all = sb("w_all", [P, 3 * C * D], F32)
        w = w_all[:, :].rearrange("p (l c d) -> p l c d", l=3, c=C)
        e_t = [w_all[:, i * 512:(i + 1) * 512] for i in range(2)]
        misc = sb("misc", [P, 3 * D], F32)
        xn = [misc[:, i * D:(i + 1) * D] for i in range(2)]
        bias_bc = misc[:, 2 * D:3 * D]
        p_t = [w_all[:, 1024:1536], misc[:, D:3 * D]]
        hs = sb("hs", [P, 4 * D], F32)
        ht = [hs[:, i * D:(i + 1) * D] for i in range(2)]
        s32 = [hs[:, (2 + i) * D:(3 + i) * D] for i in range(2)]
        p_hi = [hs[:, i * 256:(i + 1) * 256].bitcast(F16) for i in range(2)]
        p_lo = [hs[:, (2 + i) * 256:(3 + i) * 256].bitcast(F16) for i in range(2)]
        ident_f = sb("ident_f", [P, P], F32)
        ident_16 = sb("ident_16", [P, P], F16)
        one_16 = sb("one_16", [P, P], F16)
        small = sb("small", [P, 320], F32)

        taken = [0]

        def col(n):
            taken[0] += n
            return small[:, taken[0] - n:taken[0]]

        deg = col(NB)
        part = col(NB)
        row = col(NB)
        f0 = col(NB)
        dinv = col(NB)
        s1 = col(NB)
        f3 = col(NB)
        half = col(NB)
        bn = [col(6) for _ in range(2)]
        mv = [col(2) for _ in range(2)]
        ve = [col(1) for _ in range(2)]
        rstd = [col(1) for _ in range(2)]
        ss = [col(1) for _ in range(2)]
        ssm = [col(1) for _ in range(2)]
        inv = [col(1) for _ in range(2)]
        rden = col(GB)
        rsc = col(GB)
        wpart = col(4)
        wmax = col(4)
        p2 = col(3)
        p2i = col(3)
        thr = col(1)
        carrier = col(1)
        cnt = part
        tmp = deg
        assert taken[0] <= 320

        ps = ctx.enter_context(nc.psum_tensor("ps", [P, 8, 512], F32))

        block = ctx.enter_context(nc.Block())

        @block.sync
        def _(sp):
            for l, wl in enumerate((w0, w1, w2)):
                sp.dma_start(w[:, l, :, :], wl.rearrange("(c p) d -> p c d", p=P)).then_inc(sem["w_loaded"], 16)
            sp.dma_start(b0_bc, b0.partition_broadcast(P)).then_inc(sem["b_loaded"], 16)
            for i in range(4):
                q = NB // 4
                sp.dma_start(xs[:, i * q:(i + 1) * q, :], x_v[:, i * q:(i + 1) * q, :]).then_inc(x_loaded[i], 16)
            sp.dma_start(bias_bc, bias2.partition_broadcast(P)).then_inc(sem["bias_loaded"], 16)

            def load_and_store(k, u, live):
                if live(0):
                    since(sp, sem["cast_done"], k - 1)
                    sp.dma_start(stage[u], adj_v[k, :, :]).then_inc(adj_loaded[u], 16)
                if live(2):
                    sp.wait_ge(sem["at_ready0"], (k - 1) * NQ)
                    sp.dma_start(at_dram[k - 2, :, :], at16[u]).then_inc(at_stored[u], 16)

            steps(sp, NB, 2, 2, load_and_store)
            for i in range(2):
                sp.wait_ge(at_stored[i], NB // 2 * 16)
            sp.wait_ge(sem["acc_done0"], NB)
            sp.wait_ge(sem["deg_added"], NB)

            def load1(k, u, live):
                since(sp, sem["acc_done1"], k - 3)
                sp.dma_start(slot1[u], at_dram[k, :, :]).then_inc(a1_loaded[u], 16)
                if isinstance(k, int) and k == 3:
                    sp.dma_start(group[0], at_dram[0:GB, :, :].rearrange("b p (j i) -> p b j i", i=P)).then_inc(a2_loaded[0], 16)

            steps(sp, NB, 4, 0, load1)
            sp.wait_ge(sem["acc_done1"], NB)
            sp.dma_start(group[1], at_dram[GB:2 * GB, :, :].rearrange("b p (j i) -> p b j i", i=P)).then_inc(a2_loaded[1], 16)
            with sp.Fori(2, NG - 1, 2) as g0:
                for u in range(2):
                    sp.wait_ge(sem["p_done"], (g0 + u - 1) * NB)
                    src = at_dram.rearrange("(g b) p (j i) -> g p b j i", b=GB, i=P)[g0 + u, :, :, :, :]
                    sp.dma_start(group[u], src).then_inc(a2_loaded[u], 16)
            sp.wait_ge(sem["p_done"], (NG - 1) * NB)

            def load3(k, u, live):
                since(sp, sem["acc_done3"], k - 3)
                sp.dma_start(slot3[u], at_dram[k, :, :]).then_inc(a3_loaded[u], 16)

            steps(sp, NB, 4, 0, load3)

        @block.gpsimd
        def _(pool):
            pool.memset(ident_f[:, :], 0.0).then_inc(sem["ident_zero"], 1)
            pool.memset(ident_16[:, :], 0.0).then_inc(sem["ident_zero"], 1)
            pool.memset(half, -0.5).then_inc(sem["half_set"], 1)
            for i in range(2):
                pool.memset(val_hi[i][:, :, D:D + 1], 1.0).then_inc(sem["ones_set"], 1)
            pool.memset(one_16[:, :], 0.0).then_inc(sem["ident_zero"], 1)
            pool.wait_ge(sem["ident_zero"], 3)
            pool.affine_select(out=ident_f[:, :], in_=ident_f[:, :], compare_op=ALU.not_equal, fill=1.0,
                               base=0, pattern=[[-1, P]], channel_multiplier=1).then_inc(sem["ident_f"], 1)
            pool.affine_select(out=ident_16[:, :], in_=ident_16[:, :], compare_op=ALU.not_equal, fill=ASC,
                               base=0, pattern=[[-1, P]], channel_multiplier=1).then_inc(sem["ident_16"], 1)
            pool.affine_select(out=one_16[:, :], in_=one_16[:, :], compare_op=ALU.not_equal, fill=1.0,
                               base=0, pattern=[[-1, P]], channel_multiplier=1).then_inc(sem["one_16"], 1)
            pool.wait_ge(sem["wmax_part"], 4)
            pool.partition_all_reduce(wmax, wpart, P, RMAX).then_inc(sem["wmax_all"], 1)
            pool.wait_ge(sem["half_set"], 1)

            def rstds(l):
                def body(k, u, live):
                    pool.wait_ge(prep[l]["var_ready"], k + 1)
                    nc.gpsimd.tensor_tensor(rstd[u], ve[u], half[:, 0:1], ALU.pow).then_inc(prep[l]["rstd_ready"], 1)
                return body

            steps(pool, NB, 2, 0, rstds(0))
            pool.wait_ge(sem["cnt1_ready"], 1)
            nc.gpsimd.tensor_tensor(dinv, dinv, half, ALU.pow).then_inc(sem["dinv_ready"], 1)
            steps(pool, NB, 2, 0, rstds(1))
            pool.wait_ge(sem["r3_clamped"], 1)
            nc.gpsimd.tensor_tensor(f3, f3, half, ALU.pow).then_inc(sem["r3_ready"], 1)

            def powers2(k, u, live):
                rstds(2)(k, u, live)
                pool.wait_ge(sem["ss_clamped"], k + 1)
                nc.gpsimd.tensor_tensor(inv[u], ssm[u], half[:, 0:1], ALU.pow).then_inc(sem["inv_ready"], 1)

            steps(pool, NB, 2, 0, powers2)
            steps(pool, NB, 2, 0, rstds(3))

        def carry_wait():
            nc.vector.memset(carrier, 0.0)

        def row_sums(l, k, u):
            nc.vector.bn_stats(bn[u], xs[:, k, :]).then_inc(prep[l]["bn_done"], 1)

        def moments(dve, l, k, u):
            dve.wait_ge(prep[l]["bn_done"], k + 1)
            carry_wait()
            nc.vector.bn_aggr(mv[u], bn[u]).then_inc(prep[l]["aggr_done"], 1)

        def variance(dve, l, k, u, scale=1.0):
            dve.wait_ge(prep[l]["aggr_done"], k + 1)
            nc.vector.tensor_scalar(ve[u], mv[u][:, 1:2], scale, LN_EPS * scale,
                                    ALU.mult, ALU.add).then_inc(prep[l]["var_ready"], 1)

        def stats(dve, l, k, u, scale=1.0):
            carry_wait()
            row_sums(l, k, u)
            moments(dve, l, k, u)
            variance(dve, l, k, u, scale)

        def normalize(dve, l, k, u, to=None):
            to = u if to is None else to
            s = prep[l]
            dve.wait_ge(s["rstd_ready"], k + 1)
            if l < 3:
                since(dve, s["tp_done"], k - 1)
            nc.vector.tensor_scalar(xn[to], xs[:, k, :], mv[u][:, 0:1], rstd[u],
                                    ALU.subtract, ALU.mult).then_inc(s["xn_ready"], 1)

        def low_part(dve, l, k, u):
            s = prep[l]
            dve.wait_ge(s["hi_ready"], k + 1)
            nc.vector.tensor_tensor(val_lo[l % 2][:, k, :], s32[u], val_hi[l % 2][:, k, 0:D],
                                    ALU.subtract).then_inc(s["val_ready"], 1)

        @block.vector
        def _(dve):
            nc.vector.memset(deg, 0.0).then_inc(sem["deg_zero"], 1)
            dve.wait_ge(sem["w_loaded"], 48)
            for l in range(3):
                nc.vector.tensor_reduce(wpart[:, l:l + 1], w[:, l, :, :], AX.XY, ALU.max,
                                        apply_absolute_value=True).then_inc(sem["wmax_part"], 1)
            dve.wait_ge(sem["b_loaded"], 16)
            nc.vector.tensor_reduce(wpart[:, 3:4], b0_bc, AX.X, ALU.max,
                                    apply_absolute_value=True).then_inc(sem["wmax_part"], 1)
            dve.wait_ge(sem["wmax_all"], 1)
            nc.vector.tensor_tensor(wmax[:, 0:1], wmax[:, 0:1], wmax[:, 3:4], ALU.max).then_inc(sem["p2_clamped"], 1)
            dve.wait_ge(sem["p2_clamped"], 1)
            nc.vector.tensor_scalar(p2, wmax[:, 0:3], 2.0 ** -60, None, ALU.max).then_inc(sem["p2_clamped"], 1)
            dve.wait_ge(sem["p2_clamped"], 2)
            nc.vector.tensor_scalar(p2.bitcast(I32), p2.bitcast(I32), EXPONENT_BITS, None,
                                    ALU.bitwise_and).then_inc(sem["p2_masked"], 1)
            dve.wait_ge(sem["p2_masked"], 1)
            nc.vector.reciprocal(p2i, p2).then_inc(sem["p2_inv"], 1)
            dve.wait_ge(sem["p2_inv"], 1)
            nc.vector.tensor_scalar(thr, p2i[:, 2:3], NORM_EPS * VSC, None, ALU.mult).then_inc(sem["thr_step"], 1)
            dve.wait_ge(sem["thr_step"], 1)
            nc.vector.tensor_tensor(thr, thr, thr, ALU.mult).then_inc(sem["thr_step"], 1)
            for l in range(3):
                nc.vector.tensor_scalar(w[:, l, :, :], w[:, l, :, :], p2i[:, l:l + 1], VSC,
                                        ALU.mult, ALU.mult).then_inc(sem["scaled_w"], 1)
            nc.vector.tensor_scalar(b0_bc, b0_bc, p2i[:, 0:1], VSC, ALU.mult, ALU.mult).then_inc(sem["scaled_w"], 1)
            dve.wait_ge(sem["scaled_w"], 4)

            for i in range(4):
                dve.wait_ge(x_loaded[i], 16)

            def prep0(k, u, live):
                if live(0):
                    row_sums(0, k, u)
                if live(1):
                    normalize(dve, 0, k - 1, 1 - u)
                if live(0):
                    moments(dve, 0, k, u)
                if live(3):
                    dve.wait_ge(prep[0]["o_done"], k - 2)
                    since(dve, prep[0]["val_ready"], k - 4)
                    nc.vector.tensor_tensor(s32[1 - u], ps[:, 7 - u, 0:D], b0_bc, ALU.add).then_inc(prep[0]["s_ready"], 1)
                if live(0):
                    variance(dve, 0, k, u)
                if live(4):
                    low_part(dve, 0, k - 4, u)

            steps(dve, NB, 2, 4, prep0)

            dve.wait_ge(sem["deg_zero"], 1)

            def sums0(k, u, live):
                if live(0):
                    dve.wait_ge(adj_loaded[u], k * 8 + 16 - 8 * u)
                    since(dve, tq_done, (k - 1) * NQ)
                    nc.vector.tensor_copy(cast16[u], stage[u]).then_inc(sem["cast_done"], 1)
                if live(1):
                    since(dve, sem["deg_added"], k - 1)
                    dve.wait_ge(sem["at_ready0"], k * NQ)
                    nc.vector.tensor_reduce(part, at16[1 - u].rearrange("p (j i) -> p j i", i=P),
                                            AX.X, ALU.add).then_inc(sem["part_sum"], 1)
                    dve.wait_ge(sem["part_sum"], k)
                    nc.vector.tensor_tensor(deg, deg, part, ALU.add).then_inc(sem["deg_added"], 1)
                if live(2):
                    dve.wait_ge(sem["acc_done0"], k - 1)
                    nc.vector.tensor_copy(y0[:, k - 2, :], ps[:, 4 + u, 0:D])
                    nc.vector.tensor_copy(row[:, bass.ds(k - 2, 1)], ps[:, 4 + u, D:D + 1]).then_inc(sem["y_saved"], 1)

            steps(dve, NB, 2, 2, sums0)

            dve.wait_ge(sem["deg_added"], NB)
            nc.vector.reciprocal(f0, deg).then_inc(sem["f0_ready"], 1)
            dve.wait_ge(sem["y_saved"], NB)
            nc.vector.tensor_scalar(dinv, row, 1.0 / ASC, 1.0, ALU.mult, ALU.add).then_inc(sem["cnt1_ready"], 1)
            dve.wait_ge(sem["f0_ready"], 1)
            nc.vector.tensor_scalar(f0, f0, p2[:, 0:1], 1.0 / VSC, ALU.mult, ALU.mult).then_inc(sem["f0_ready"], 1)
            dve.wait_ge(sem["f0_ready"], 2)

            def prep1(k, u, live):
                if live(0):
                    nc.vector.scalar_tensor_tensor(xs[:, k, :], y0[:, k, :], f0[:, bass.ds(k, 1)], xs[:, k, :],
                                                   ALU.mult, ALU.add).then_inc(sem["x1_ready"], 1)
                if live(1):
                    normalize(dve, 1, k - 1, 1 - u)
                if live(0):
                    dve.wait_ge(sem["x1_ready"], k + 1)
                    carry_wait()
                    row_sums(1, k, u)
                if live(0):
                    moments(dve, 1, k, u)
                if live(3):
                    low_part(dve, 1, k - 3, 1 - u)
                if live(0):
                    variance(dve, 1, k, u)

            steps(dve, NB, 2, 3, prep1)

            nc.vector.tensor_scalar(cnt, row, 1.0 / ASC, None, ALU.mult).then_inc(sem["cnt_ready"], 1)
            dve.wait_ge(sem["cnt_ready"], 1)
            nc.vector.tensor_scalar(f3, cnt, HEAD_EPS ** 2, None, ALU.max).then_inc(sem["r3_clamped"], 1)
            dve.wait_ge(sem["dinv_ready"], 1)
            nc.vector.tensor_scalar(s1, dinv, p2[:, 1:2], 1.0 / (ASC * VSC), ALU.mult, ALU.mult).then_inc(sem["s1_ready"], 1)
            dve.wait_ge(sem["r3_ready"], 1)
            nc.vector.tensor_scalar(f3, f3, 1.0, None, ALU.add).then_inc(sem["f3_a"], 1)
            dve.wait_ge(sem["f3_a"], 1)
            nc.vector.tensor_tensor(tmp, cnt, f3, ALU.mult).then_inc(sem["f3_b"], 1)
            dve.wait_ge(sem["f3_b"], 1)
            nc.vector.reciprocal(tmp, tmp).then_inc(sem["f3_c"], 1)
            dve.wait_ge(sem["f3_c"], 1)
            nc.vector.scalar_tensor_tensor(f3, f3, 1.0 / (ASC * VSC), tmp, ALU.mult, ALU.mult).then_inc(sem["f3_ready"], 1)
            dve.wait_ge(sem["s1_ready"], 1)
            dve.wait_ge(sem["f3_ready"], 1)

            def layer1(k, u, live):
                if live(0):
                    dve.wait_ge(sem["acc_done1"], k + 1)
                    since(dve, sem["hn_ready"], k - 1)
                    nc.vector.tensor_scalar(xn[u], ps[:, u, 0:D], s1[:, bass.ds(k, 1)], 0.0,
                                            ALU.mult, ALU.max).then_inc(sem["relu1"], 1)
                    dve.wait_ge(sem["relu1"], k + 1)
                    nc.vector.tensor_tensor(xs[:, k, :], xs[:, k, :], xn[u], ALU.add).then_inc(sem["epi_done1"], 1)
                    dve.wait_ge(sem["epi_done1"], k + 1)
                    stats(dve, 2, k, u)
                if live(1):
                    dve.wait_ge(sem["hnhi_ready"], k)
                    nc.vector.tensor_tensor(hnt[:, 1, :, bass.ds((k - 1) * P, P)], ps[:, 5, 0:D].rearrange("p (c i) -> p c i", c=C),
                                            hnt[:, 0, :, bass.ds((k - 1) * P, P)], ALU.subtract).then_inc(sem["hnt_ready"], 1)
                if live(0):
                    normalize(dve, 2, k, u)
                    dve.wait_ge(prep[2]["xn_ready"], k + 1)
                    nc.vector.tensor_tensor(xs[:, k, :], xs[:, k, :], bias_bc, ALU.add).then_inc(sem["x_biased"], 1)
                    dve.wait_ge(prep[2]["s_ready"], k + 1)
                    nc.vector.tensor_copy(val_hi[0][:, k, 0:D], s32[u]).then_inc(prep[2]["hi_ready"], 1)
                    dve.wait_ge(sem["sumsq_ready"], k + 1)
                    nc.vector.tensor_tensor(ssm[u], ss[u], thr, ALU.max).then_inc(sem["ss_clamped"], 1)
                    low_part(dve, 2, k, u)
                    dve.wait_ge(sem["inv_ready"], k + 1)
                    dve.wait_ge(prep[2]["val_ready"], k + 1)
                    nc.vector.tensor_scalar(s32[u], s32[u], inv[u], VSC, ALU.mult, ALU.mult).then_inc(sem["hn_ready"], 1)

            dve.wait_ge(sem["bias_loaded"], 16)
            dve.wait_ge(sem["thr_step"], 2)
            steps(dve, NB, 2, 1, layer1)

            def results2(g):
                dve.wait_ge(sem["pv_done"], (g + 1) * NB)
                for b in range(GB):
                    nc.vector.reciprocal(rden[:, b:b + 1], ps[:, b, D:D + 1]).then_inc(sem["rden_ready"], 1)
                dve.wait_ge(sem["rden_ready"], (g + 1) * GB)
                nc.vector.tensor_scalar(rsc, rden, p2[:, 2:3], 1.0 / VSC, ALU.mult, ALU.mult).then_inc(sem["rsc_ready"], 1)
                dve.wait_ge(sem["rsc_ready"], g + 1)
                for b in range(GB):
                    nc.vector.scalar_tensor_tensor(xs[:, g * GB + b, :], ps[:, b, 0:D], rsc[:, b:b + 1],
                                                   xs[:, g * GB + b, :], ALU.mult, ALU.add).then_inc(sem["epi_done2"], 1)

            def prep3(g, b):
                k, u, s = g * GB + b, b % 2, prep[3]
                dve.wait_ge(sem["epi_done2"], k + 1 + GB)
                since(dve, s["val_ready"], k)
                stats(dve, 3, k, u, 1.0 / VSC ** 2)
                normalize(dve, 3, k, u, 0)
                dve.wait_ge(s["xn_ready"], k + 1)
                nc.vector.tensor_scalar(val_hi[1][:, k, 0:D], xn[0], 0.0, None, ALU.max).then_inc(s["hi_ready"], 1)
                dve.wait_ge(s["hi_ready"], k + 1)
                nc.vector.scalar_tensor_tensor(val_lo[1][:, k, :], xn[0], 0.0, val_hi[1][:, k, 0:D],
                                               ALU.max, ALU.subtract).then_inc(s["val_ready"], 1)

            def weights(g, gu, j):
                n, u = g * NB + j, j % 2
                if j == 0:
                    dve.wait_ge(a2_loaded[gu], g * 8 + 16 - 8 * gu)
                since(dve, sem["p_ready"], n - 1)
                dve.wait_ge(sem["exp_done"], n + 1)
                nc.vector.scalar_tensor_tensor(p_t[u].rearrange("p (b i) -> p b i", i=P), group[gu][:, :, j, :],
                                               ATTN_EPS * ASC, e_t[u].rearrange("p (b i) -> p b i", i=P),
                                               ALU.add, ALU.mult).then_inc(sem["p_done"], 1)

            def attention(g, gu, first):
                for j in range(1, NB + 1):
                    n, u = g * NB + j, j % 2
                    if j < NB:
                        weights(g, gu, j)
                    elif not (isinstance(g, int) and g == NG - 1):
                        weights(g + 1, 1 - gu, 0)
                    if j >= 1:
                        if j >= 3:
                            dve.wait_ge(sem["pv_done"], n - 2)
                        dve.wait_ge(sem["phi_done"], n)
                        nc.vector.tensor_tensor(p_lo[1 - u], p_t[1 - u], p_hi[1 - u], ALU.subtract).then_inc(sem["p_ready"], 1)
                    if j % 8 == 7 and not first:
                        prep3(g - 1, j // 8)
                results2(g)

            dve.sem_inc(sem["epi_done2"], GB)
            weights(0, 0, 0)
            attention(0, 0, True)
            attention(1, 1, False)
            with dve.Fori(2, NG - 3, 2) as g0:
                for gu in range(2):
                    attention(g0 + gu, gu, False)
            attention(NG - 2, 0, False)
            attention(NG - 1, 1, False)
            for b in range(GB):
                prep3(NG - 1, b)

            def layer3(k, u, live):
                dve.wait_ge(sem["acc_done3"], k + 1)
                nc.vector.scalar_tensor_tensor(xs[:, k, :], ps[:, 4 + u, 0:D], f3[:, bass.ds(k, 1)], xs[:, k, :],
                                               ALU.mult, ALU.add).then_inc(sem["epi_done3"], 1)

            steps(dve, NB, 2, 0, layer3)

        @block.scalar
        def _(act):
            def relu(l, k, u, bank):
                s = prep[l]
                act.wait_ge(s["tp_done"], k + 1)
                since(act, s["o_done"], k - 1)
                nc.scalar.activation(ht[u], ps[:, bank, 0:D], ACT.Relu).then_inc(s["ht_ready"], 1)

            def prep0(k, u, live):
                if live(0):
                    relu(0, k, u, 4 + u)
                if live(2):
                    act.wait_ge(prep[0]["s_ready"], k - 1)
                    nc.scalar.activation(val_hi[0][:, k - 2, 0:D], s32[u], ACT.Copy).then_inc(prep[0]["hi_ready"], 1)

            steps(act, NB, 2, 2, prep0)

            def tiles0(k, u, live):
                for q in range(NQ):
                    act.wait_ge(tq_done, k * NQ + q + 1)
                    if q == 0:
                        since(act, sem["acc_done0"], k - 1)
                        since(act, sem["part_sum"], k - 1)
                        if not (isinstance(k, int) and k < 2):
                            act.wait_ge(at_stored[u], k * 8 - 8 * u)
                    nc.scalar.activation(at16[u][:, q * TQ * P:(q + 1) * TQ * P],
                                         ps[:, q % 4, :].bitcast(F16), ACT.Copy,
                                         scale=ASC).then_inc(sem["at_ready0"], 1)

            steps(act, NB, 2, 0, tiles0)

            def prep1(k, u, live):
                if live(0):
                    relu(1, k, u, 4 + u)
                if live(1):
                    if isinstance(k, int) and k == 1:
                        act.wait_ge(sem["dinv_ready"], 1)
                    act.wait_ge(prep[1]["o_done"], k)
                    since(act, prep[1]["val_ready"], k - 2)
                    nc.scalar.activation(s32[1 - u], ps[:, 7 - u, 0:D], ACT.Copy,
                                         scale=dinv[:, bass.ds(k - 1, 1)]).then_inc(prep[1]["s_ready"], 1)
                if live(1):
                    act.wait_ge(prep[1]["s_ready"], k)
                    nc.scalar.activation(val_hi[1][:, k - 1, 0:D], s32[1 - u], ACT.Copy).then_inc(prep[1]["hi_ready"], 1)

            steps(act, NB, 2, 1, prep1)

            def layer1(k, u, live):
                if live(1):
                    act.wait_ge(sem["tn_done"], k)
                    nc.scalar.activation(hnt[:, 0, :, bass.ds((k - 1) * P, P)], ps[:, 5, 0:D].rearrange("p (c i) -> p c i", c=C),
                                         ACT.Copy).then_inc(sem["hnhi_ready"], 1)
                if live(0):
                    relu(2, k, u, 4)
                    act.wait_ge(prep[2]["o_done"], k + 1)
                    since(act, sem["tn_done"], k - 1)
                    nc.scalar.activation(s32[u], ps[:, 6, 0:D], ACT.Copy).then_inc(prep[2]["s_ready"], 1)
                    act.wait_ge(prep[2]["s_ready"], k + 1)
                    nc.scalar.activation(ps[:, 6, 0:D], ps[:, 6, 0:D], ACT.Square, accum_out=ss[u]).then_inc(sem["sumsq_ready"], 1)

            steps(act, NB, 2, 1, layer1)

            def exps(k, u, live):
                if live(0):
                    act.wait_ge(sem["s_done"], k + 1)
                    since(act, sem["p_done"], k - 1)
                    nc.scalar.activation(e_t[u % 2], ps[:, 4 + u, :], ACT.Exp, scale=1.0 / VSC ** 2).then_inc(sem["exp_done"], 1)
                if live(1):
                    act.wait_ge(sem["p_done"], k)
                    since(act, sem["pv_done"], k - 2)
                    nc.scalar.activation(p_hi[(u + 1) % 2], p_t[(u + 1) % 2], ACT.Copy).then_inc(sem["phi_done"], 1)

            steps(act, NG * NB, 4, 1, exps)

            def store(k, u, live):
                act.wait_ge(sem["epi_done3"], k + 1)
                act.dma_start(out_v[k, :, :], xs[:, k, :]).then_inc(sem["out_stored"], 16)

            steps(act, NB, 2, 0, store)
            act.wait_ge(sem["out_stored"], NB * 16)

        @block.tensor
        def _(pe):
            def transposes(l, k, u, bank, lag):
                s = prep[l]
                pe.wait_ge(s["xn_ready"], k + 1)
                since(pe, s["ht_ready"], k - lag + 1)
                for c in range(C):
                    last = nc.tensor.transpose(ps[:, bank, c * P:(c + 1) * P], xn[u][:, c * P:(c + 1) * P], ident_f[:, :])
                last.then_inc(s["tp_done"], 1)

            def project(l, k, u, bank, free, freed):
                s = prep[l]
                pe.wait_ge(s["ht_ready"], k + 1)
                since(pe, free, freed)
                for c in range(C):
                    last = nc.tensor.matmul(ps[:, bank, 0:D], ht[u][:, c * P:(c + 1) * P], w[:, l, c, :],
                                            start=(c == 0), stop=(c == C - 1))
                last.then_inc(s["o_done"], 1)

            def prepare(l):
                def body(k, u, live):
                    if live(0):
                        transposes(l, k, u, 4 + u, 2)
                    if live(1):
                        project(l, k - 1, 1 - u, 7 - u, prep[l]["s_ready"], k - 2)
                return body

            def block_sum(bank, at, v, j, start, stop):
                nc.tensor.matmul(ps[:, bank, 0:D + 1], at, val_hi[v][:, j, 0:D + 1], start=start, stop=False)
                return nc.tensor.matmul(ps[:, bank, 0:D], at, val_lo[v][:, j, :], start=False, stop=stop)

            pe.wait_ge(sem["ident_f"], 1)
            pe.wait_ge(sem["scaled_w"], 4)
            steps(pe, NB, 2, 1, prepare(0))

            def values(l, k, j):
                if isinstance(k, int) and k == 0:
                    pe.wait_ge(prep[l]["val_ready"], j + 1)

            pe.wait_ge(sem["ones_set"], 2)
            pe.wait_ge(sem["one_16"], 1)

            def layer0(k, u, live):
                for q in range(NQ):
                    if live(0):
                        if q == 0:
                            pe.wait_ge(sem["cast_done"], k + 1)
                        since(pe, sem["at_ready0"], k * NQ + q - 3)
                        for r in range(TQ):
                            j = q * TQ + r
                            last = nc.tensor.transpose(ps[:, q % 4, :].bitcast(F16)[:, r * P:(r + 1) * P],
                                                       cast16[u][:, j * P:(j + 1) * P], one_16[:, :])
                        last.then_inc(tq_done, 1)
                    if live(1):
                        pe.wait_ge(sem["at_ready0"], (k - 1) * NQ + q + 1)
                        if q == 0:
                            since(pe, sem["y_saved"], k - 2)
                        for r in range(TQ):
                            j = q * TQ + r
                            values(0, k - 1, j)
                            last = block_sum(5 - u, at16[1 - u][:, j * P:(j + 1) * P], 0, j, j == 0, j == NB - 1)
                        if q == NQ - 1:
                            last.then_inc(sem["acc_done0"], 1)

            steps(pe, NB, 2, 1, layer0)

            steps(pe, NB, 2, 1, prepare(1))
            pe.wait_ge(sem["ident_16"], 1)

            def transpose_unit(k, u):
                pe.wait_ge(sem["hn_ready"], k + 1)
                since(pe, sem["hnt_ready"], k)
                for c in range(C):
                    last = nc.tensor.transpose(ps[:, 5, c * P:(c + 1) * P], s32[u][:, c * P:(c + 1) * P], ident_f[:, :])
                last.then_inc(sem["tn_done"], 1)

            def layer1(k, u4, live):
                u = u4 % 2
                if live(0):
                    pe.wait_ge(a1_loaded[u4], k * 4 + 16 - 4 * u4)
                    since(pe, sem["epi_done1"], k - 1)
                for j in range(NB):
                    if live(0):
                        values(1, k, j)
                        block_sum(u, slot1[u4][:, j * P:(j + 1) * P], 1, j, j == 0, False)
                    if j == 8 and live(2):
                        transpose_unit(k - 2, u)
                    if j == 18 and live(1):
                        transposes(2, k - 1, 1 - u, 4, 1)
                    if j == 25 and live(1):
                        project(2, k - 1, 1 - u, 6, sem["sumsq_ready"], k - 1)
                if live(0):
                    block_sum(u, ident_16[:, :], 1, k, False, True).then_inc(sem["acc_done1"], 1)

            steps(pe, NB, 4, 2, layer1)

            pe.wait_ge(sem["hnt_ready"], NB)
            pe.wait_ge(prep[2]["val_ready"], NB)

            def scores(g, j):
                n, bank = g * NB + j, 4 + j % 4
                if j != 3:
                    since(pe, sem["exp_done"], n - 3)
                passes = [(0, 0), (0, 1), (1, 0)]
                for c in range(C):
                    for a, b in passes:
                        last = nc.tensor.matmul(ps[:, bank, :], hnt[:, a, c, j * P:(j + 1) * P],
                                                hnt[:, b, c, bass.ds(g * GB * P, GB * P)],
                                                start=(c == 0 and (a, b) == (0, 0)),
                                                stop=(c == C - 1 and (a, b) == (1, 0)))
                last.then_inc(sem["s_done"], 1)

            def weighted(g, j):
                n, u = g * NB + j, j % 2
                pe.wait_ge(sem["p_ready"], n + 1)
                for b in range(GB):
                    if j == 0:
                        pe.wait_ge(sem["epi_done2"], g * GB + b + 1)
                    block_sum(b, p_hi[u][:, b * P:(b + 1) * P], 0, j, j == 0, False)
                    last = nc.tensor.matmul(ps[:, b, 0:D + 1], p_lo[u][:, b * P:(b + 1) * P], val_hi[0][:, j, 0:D + 1],
                                            start=False, stop=(j == NB - 1))
                last.then_inc(sem["pv_done"], 1)

            def attend(g, last):
                for j in range(NB):
                    if j + 3 < NB:
                        scores(g, j + 3)
                    elif not last:
                        scores(g + 1, j + 3 - NB)
                    weighted(g, j)

            scores(0, 0)
            scores(0, 1)
            scores(0, 2)
            with pe.Fori(0, NG - 1, 1) as g:
                attend(g, False)
            attend(NG - 1, True)

            def layer3(k, u4, live):
                u = u4 % 2
                pe.wait_ge(a3_loaded[u4], k * 4 + 16 - 4 * u4)
                since(pe, sem["epi_done3"], k - 1)
                for j in range(NB):
                    values(3, k, j)
                    last = block_sum(4 + u, slot3[u4][:, j * P:(j + 1) * P], 1, j, j == 0, j == NB - 1)
                last.then_inc(sem["acc_done3"], 1)

            steps(pe, NB, 4, 0, layer3)


_INS = ['x', 'adj', 'L0_gnn_W', 'L0_gnn_b', 'L1_gnn_weight', 'L2_gnn_weight', 'L2_gnn_bias']


def kernel(**inputs):
    import numpy as _np
    import concourse.bacc as _bacc
    from concourse import mybir as _mybir
    from concourse.bass_utils import run_bass_kernel_spmd as _run

    nc = _bacc.Bacc("TRN2", target_bir_lowering=False, num_devices=1)
    arrays, args = {}, []
    for name in _INS:
        a = _np.ascontiguousarray(inputs[name])
        arrays[f"in_{name}"] = a
        args.append(nc.dram_tensor(f"in_{name}", a.shape, _mybir.dt.from_np(a.dtype), kind="ExternalInput").ap())
    out = nc.dram_tensor("out", inputs["x"].shape, _mybir.dt.float32, kind="ExternalOutput").ap()
    gnn_kernel(nc, *args, out)
    r = _run(nc, [arrays], core_ids=[0])
    return r.results[0]["out"]
```
